# Optimizing a Trainium2 kernel written in Bass

```python
import numpy as np
import jax
import jax.numpy as jnp

def _softmax(x, axis=-1):
    return jax.nn.softmax(x, axis=axis)

def _gelu(x):
    return jax.nn.gelu(x, approximate=True)

def _silu(x):
    return jax.nn.silu(x)

def _sigmoid(x):
    return jax.nn.sigmoid(x)

def _layernorm(x, axis=-1, eps=1e-05):
    m = jnp.mean(x, axis=axis, keepdims=True)
    v = jnp.var(x, axis=axis, keepdims=True)
    return (x - m) / jnp.sqrt(v + eps)

def _scatter_add(tgt, idx, src, axis=0):
    return tgt.at[idx].add(src)

def _segment_sum(src, seg, n):
    return jax.ops.segment_sum(src, seg, n)
kernel_name = 'mk_gnn_resnorm_d2_gnn_r8_540b69'

def setup_inputs(seed: int=0):
    np.random.seed(seed)
    _w = jnp.asarray

    def _rec_inputs():
        import jax
        import jax.numpy as jnp
        _gk = jax.random.key(seed)
        x = -0.0001079 + 1 * jax.random.normal(jax.random.fold_in(_gk, 1), (12500, 32), jnp.float32)
        _s = jax.random.randint(jax.random.fold_in(_gk, 2), (100000,), 0, 12500, jnp.int32)
        _d = jax.random.randint(jax.random.fold_in(_gk, 3), (100000,), 0, 12500, jnp.int32)
        _loop = jnp.arange(12500, dtype=jnp.int32)
        src = jnp.concatenate([_s, _d, _loop])
        dst = jnp.concatenate([_d, _s, _loop])
        _o = jnp.argsort(dst, stable=True)
        src = src[_o]
        dst = dst[_o]
        edge_attr_32 = 0.000216709 + 1.00012 * jax.random.normal(jax.random.fold_in(_gk, 11), (212500, 32), jnp.float32)
        edge_attr_4 = 0.000714719 + 1.00021 * jax.random.normal(jax.random.fold_in(_gk, 12), (212500, 4), jnp.float32)
        return (x, src, dst, edge_attr_32, edge_attr_4)
    x, src, dst, edge_attr_32, edge_attr_4 = _rec_inputs()

    def _L0_gnn_setup():
        import jax, jax.numpy as jnp
        import numpy as np
        NUM_NODES = 12500
        EMB_DIM = 32
        NUM_EDGES = 200000
        key = jax.random.key(seed)
        k1, k2 = jax.random.split(key)
        edge_index = jax.random.randint(k1, (2, NUM_EDGES), 0, NUM_NODES, dtype=jnp.int64)
        embedding_weight = jax.random.normal(k2, (NUM_NODES, EMB_DIM), dtype=jnp.float32)
        return {'edge_index': edge_index, 'embedding_weight': embedding_weight}
    _L0_gnn_all = _L0_gnn_setup()
    _L0_gnn_in = {k: v for k, v in _L0_gnn_all.items() if k in ()}
    del _L0_gnn_all

    def _L1_gnn_setup():
        import jax, jax.numpy as jnp
        import numpy as np
        MUL = 8
        N_NODES = 12500
        N_EDGES = 100000
        EDGE_DIM = 32
        MLP_DIM = 64
        W_NUMEL = 4 * MUL * MUL
        ALPHA = 0.25
        C110 = 1.0 / np.sqrt(3.0)
        SI_SCALE = 1.0 / np.sqrt(MUL)
        key = jax.random.key(seed)
        ks = jax.random.split(key, 10)
        node_attr = jax.random.normal(ks[0], (N_NODES, 4 * MUL), dtype=jnp.float32)
        edge_index = jax.random.randint(ks[1], (2, N_EDGES), 0, N_NODES, dtype=jnp.int64)
        edge_sh = jax.random.normal(ks[2], (N_EDGES, 4), dtype=jnp.float32)
        edge_feat = jax.random.normal(ks[3], (N_EDGES, EDGE_DIM), dtype=jnp.float32)
        W1 = jax.random.normal(ks[4], (EDGE_DIM, MLP_DIM), dtype=jnp.float32) / np.sqrt(EDGE_DIM)
        b1 = jnp.zeros((MLP_DIM,), dtype=jnp.float32)
        W2 = jax.random.normal(ks[5], (MLP_DIM, W_NUMEL), dtype=jnp.float32) / np.sqrt(MLP_DIM)
        b2 = jnp.zeros((W_NUMEL,), dtype=jnp.float32)
        si_w0 = jax.random.normal(ks[6], (MUL, MUL), dtype=jnp.float32)
        si_w1 = jax.random.normal(ks[7], (MUL, MUL), dtype=jnp.float32)
        return {'node_attr': node_attr, 'edge_index': edge_index, 'edge_sh': edge_sh, 'edge_feat': edge_feat, 'W1': W1, 'b1': b1, 'W2': W2, 'b2': b2, 'si_w0': si_w0, 'si_w1': si_w1}
    _L1_gnn_all = _L1_gnn_setup()
    _L1_gnn_in = {k: v for k, v in _L1_gnn_all.items() if k in ('W1', 'b1', 'W2', 'b2', 'si_w0', 'si_w1')}
    del _L1_gnn_all
    return {'x': x, 'src': src, 'dst': dst, 'edge_attr_32': edge_attr_32, 'edge_attr_4': edge_attr_4, 'L1_gnn_W1': _L1_gnn_in['W1'], 'L1_gnn_b1': _L1_gnn_in['b1'], 'L1_gnn_W2': _L1_gnn_in['W2'], 'L1_gnn_b2': _L1_gnn_in['b2'], 'L1_gnn_si_w0': _L1_gnn_in['si_w0'], 'L1_gnn_si_w1': _L1_gnn_in['si_w1']}

def reference(x, src, dst, edge_attr_32, edge_attr_4, L1_gnn_W1, L1_gnn_b1, L1_gnn_W2, L1_gnn_b2, L1_gnn_si_w0, L1_gnn_si_w1):
    import jax
    import jax.numpy as jnp

    def _L0_gnn_ref(edge_index, embedding_weight):
        import jax, jax.numpy as jnp
        import numpy as np
        NUM_NODES = 12500
        EMB_DIM = 32
        NUM_EDGES = 200000
        row, col = (edge_index[0], edge_index[1])
        n = embedding_weight.shape[0]
        ones = jnp.ones(row.shape[0], dtype=embedding_weight.dtype)
        deg = jax.ops.segment_sum(ones, col, num_segments=n)
        deg_inv_sqrt = jnp.where(deg > 0, jax.lax.rsqrt(jnp.maximum(deg, 1.0)), 0.0)
        norm = deg_inv_sqrt[row] * deg_inv_sqrt[col]
        msgs = embedding_weight[row] * norm[:, None]
        out = jax.ops.segment_sum(msgs, col, num_segments=n)
        return out

    def _L1_gnn_ref(node_attr, edge_index, edge_sh, edge_feat, W1, b1, W2, b2, si_w0, si_w1):
        import jax, jax.numpy as jnp
        import numpy as np
        MUL = 8
        N_NODES = 12500
        N_EDGES = 100000
        EDGE_DIM = 32
        MLP_DIM = 64
        W_NUMEL = 4 * MUL * MUL
        ALPHA = 0.25
        C110 = 1.0 / np.sqrt(3.0)
        SI_SCALE = 1.0 / np.sqrt(MUL)
        n = node_attr.shape[0]
        e = edge_sh.shape[0]
        h = jax.nn.relu(edge_feat @ W1 + b1)
        w = (h @ W2 + b2).reshape(e, 4, MUL, MUL)
        w_000, w_011, w_101, w_110 = (w[:, 0], w[:, 1], w[:, 2], w[:, 3])
        s = node_attr[:, :MUL]
        v = node_attr[:, MUL:].reshape(n, MUL, 3)
        src, dst = (edge_index[0], edge_index[1])
        s_e = s[src]
        v_e = v[src]
        sh0 = edge_sh[:, 0]
        sh1 = edge_sh[:, 1:4]
        m0 = ALPHA * (jnp.einsum('ei,eio->eo', s_e * sh0[:, None], w_000) + C110 * jnp.einsum('eim,em,eio->eo', v_e, sh1, w_110))
        m1 = ALPHA * (jnp.einsum('ei,em,eio->eom', s_e, sh1, w_011) + jnp.einsum('eim,eio->eom', v_e * sh0[:, None, None], w_101))
        out0 = jax.ops.segment_sum(m0, dst, num_segments=n)
        out1 = jax.ops.segment_sum(m1.reshape(e, MUL * 3), dst, num_segments=n).reshape(n, MUL, 3)
        out0 = out0 + SI_SCALE * (s @ si_w0)
        out1 = out1 + SI_SCALE * jnp.einsum('nim,io->nom', v, si_w1)
        return jnp.concatenate([out0, out1.reshape(n, MUL * 3)], axis=-1)
    edge_index = jnp.stack([src, dst])
    x = _layernorm(x + _L0_gnn_ref(edge_index, x), axis=-1)
    x = _layernorm(x + _L1_gnn_ref(x, edge_index, edge_attr_4, edge_attr_32, L1_gnn_W1, L1_gnn_b1, L1_gnn_W2, L1_gnn_b2, L1_gnn_si_w0, L1_gnn_si_w1), axis=-1)
    return x

_drawn_inputs = setup_inputs


def setup_inputs(seed=0):
    import zlib

    import numpy as np

    out = dict(_drawn_inputs(seed))
    spreads = {'L1_gnn_b1': (0.0, 0.1), 'L1_gnn_b2': (0.0, 0.1)}
    factors = {}
    for name, (base, spread) in spreads.items():
        noise = np.random.default_rng([zlib.crc32(name.encode()), seed]).standard_normal(out[name].shape)
        drawn = base * np.exp(spread * noise) if base else spread * noise
        out[name] = jnp.asarray(drawn.astype(out[name].dtype))
    for name, factor in factors.items():
        out[name] = (out[name] * factor).astype(out[name].dtype)
    return out
```

```python
from contextlib import ExitStack

import concourse.bass as bass
from concourse import mybir

F32 = mybir.dt.float32
BF16 = mybir.dt.bfloat16
I32 = mybir.dt.int32
ALU = mybir.AluOpType
ACT = mybir.ActivationFunctionType
AX_X = mybir.AxisListType.X
RMAX = bass.bass_isa.ReduceOp.max

P = 128
TPG = 4
GPC = 4
TPC = TPG * GPC
WIN = 64
WIDE = 512
D = 32
MUL = 8
HID = 64
WN = 4 * MUL * MUL
ALPHA = 0.25
C110 = 1.0 / 3.0 ** 0.5
SI_SCALE = 1.0 / MUL ** 0.5
EPS = 1e-5


def gnn_program(nc, x_d, src_d, dst_d, first_d, efT_d, sh_d, w1_d, b1_d, w2_d, si_d, out_d):
    n_out = out_d.shape[0]
    NPAD = x_d.shape[0]
    NP = NPAD // P
    CHUNKS = src_d.shape[0]
    TILES = CHUNKS * TPC
    GROUPS = CHUNKS * GPC
    WIDES = -(-(n_out + WIN) // WIDE)
    SUMW = WIDES * WIDE
    NC = P
    PIECES = 8
    CPP = NC // PIECES
    PW = CPP * D
    BPP = PW // P
    PAIRS = CHUNKS // 2
    assert CHUNKS % 2 == 0 and n_out + WIN <= SUMW and PW == 512

    ctx = ExitStack()
    with ctx:
        def sb(name, shape, dt=F32):
            return ctx.enter_context(nc.sbuf_tensor(name, shape, dt))

        def sem(name):
            return ctx.enter_context(nc.semaphore(name))

        y_d = nc.dram_tensor("scaled_x_table", (NPAD, D), F32).ap()
        x1_d = nc.dram_tensor("x1_table", (NPAD, D), F32).ap()

        x_sb = sb("x_sb", [P, NC, D])
        z_sb = sb("z_sb", [P, NC, D])
        q_sb = sb("q_sb", [P, NC, D])
        sumT = sb("sumT", [D, SUMW])
        deg = sb("deg", [P, NC])
        root = sb("root", [P, NC])
        dinv = sb("dinv", [P, NC])
        mean = sb("mean", [P, NC])
        var = sb("var", [P, NC])
        x1T = sb("x1T", [P, 2, BPP, P])

        dst_i = sb("dst_i", [P, TILES], I32)
        dst_f = sb("dst_f", [P, TILES])
        rel = sb("rel", [P, TILES])
        part_i = sb("part_i", [P, TILES], I32)
        hi = sb("hi", [P, TILES], BF16)
        lo = sb("lo", [P, TILES], BF16)
        first_i = sb("first_i", [P, GROUPS], I32)
        first_f = sb("first_f", [P, GROUPS])

        lane = sb("lane", [P, NC, TPC], BF16)
        lane_i = sb("lane_i", [P, WIDE], I32)
        lane_f = sb("lane_f", [P, WIDE])
        ident = sb("ident", [P, P])
        zero_b = sb("zero_b", [P, P], BF16)
        eps = sb("eps", [P, 1])
        w1 = sb("w1", [P, GPC, HID])
        b1 = sb("b1", [HID, 1])
        w2 = sb("w2", [P, WN])
        si = sb("si", [P, P])
        span = sb("span", [P, 2])
        spans = sb("spans", [P, 2])
        near_f = sb("near_f", [P, 3])
        near = sb("near", [P, 1], I32)

        idx = [sb(f"idx{k}", [P, TPC], I32) for k in range(2)]
        xg = [sb(f"xg{k}", [P, TPC, D]) for k in range(2)]
        sh = [sb(f"sh{k}", [P, TPC, 4]) for k in range(2)]
        efT = [sb(f"efT{k}", [P, TPG * P]) for k in range(2)]
        oh = [sb(f"oh{k}", [P, TPC, WIN]) for k in range(2)]
        feat = [sb(f"feat{k}", [P, TPC, 3 * MUL]) for k in range(2)]
        vec = sb("vec", [P, TPC, 3 * MUL])
        dots = sb("dots", [P, TPC, MUL, 3])
        turned = sb("turned", [P, TPC, MUL, 3])
        hT = [sb(f"hT{b}", [P, TPG * P]) for b in range(2)]
        prod = [sb(f"prod{b}", [P, TPG, 6, MUL, MUL]) for b in range(2)]
        red = sb("red", [P, TPC, 6, MUL])
        msg = [sb(f"msg{k}", [P, TPC, D]) for k in range(2)]
        wide_lane = sb("wide_lane", [P, WIDE])
        wide_oh = prod[0][:, :, :, :, :].rearrange("p t b i o -> p (t b i o)")[:, 0:2 * WIDE].rearrange(
            "p (t w) -> p t w", t=2)
        ohhi = z_sb[:, 0:64, :].rearrange("p c f -> p (c f)").bitcast(BF16)
        ohlo = q_sb[:, 0:64, :].rearrange("p c f -> p (c f)").bitcast(BF16)

        ps = ctx.enter_context(nc.psum_tensor("ps", [P, 8, 512], F32))
        ps_w = [ps[:, 2 * b:2 * b + 2, :].rearrange("p a (t n) -> p (a t) n", t=2) for b in range(2)]
        ps_h = [ps[:, 4 + b, :] for b in range(2)]
        ps_sum = ps[0:D, 6:8, 0:GPC * WIN].rearrange("p k (j w) -> p k j w", j=GPC)
        ps_wide = ps[0:D, 7, :]
        ps_deg = ps[0:NP, 7, 0:NC]

        s_in = sem("s_in")
        s_xin = sem("s_xin")
        s_win = sem("s_win")
        s_pool_c = sem("s_pool_c")
        s_dve_c = sem("s_dve_c")
        s_offsets = sem("s_offsets")
        s_maxdeg = sem("s_maxdeg")
        s_scaled = sem("s_scaled")
        s_span = sem("s_span")
        s_near = sem("s_near")
        s_doh = sem("s_doh")
        s_dmm = sem("s_dmm")
        s_degree = sem("s_degree")
        s_root = sem("s_root")
        s_w2x = sem("s_w2x")
        s_table = [sem("s_y_table"), sem("s_x1_table")]
        s_idx = [[sem(f"s_idx{l}_{k}") for k in range(2)] for l in range(2)]
        s_begun = [sem(f"s_begun{l}") for l in range(2)]
        s_edge = [sem(f"s_edge{k}") for k in range(2)]
        s_g = [[sem(f"s_g{l}_{q}") for q in range(2 * GPC)] for l in range(2)]
        s_oh = [sem(f"s_oh{l}") for l in range(2)]
        s_sum = [sem(f"s_sum{l}") for l in range(2)]
        s_acc = [sem(f"s_acc{l}") for l in range(2)]
        s_woh = [sem(f"s_woh{l}") for l in range(2)]
        s_wmm = [sem(f"s_wmm{l}") for l in range(2)]
        s_wadd = [sem(f"s_wadd{l}") for l in range(2)]
        s_zero = sem("s_zero")
        s_tr = [sem(f"s_tr{l}") for l in range(2)]
        s_ld = [sem(f"s_ld{l}") for l in range(2)]
        s_node = [sem(f"s_node{l}") for l in range(2)]
        s_cen = [sem(f"s_cen{l}") for l in range(2)]
        s_sq = [sem(f"s_sq{l}") for l in range(2)]
        s_var = [sem(f"s_var{l}") for l in range(2)]
        s_std = [sem(f"s_std{l}") for l in range(2)]
        s_row = [sem(f"s_row{l}") for l in range(2)]
        s_xt = sem("s_xt")
        s_xtc = sem("s_xtc")
        s_si = sem("s_si")
        s_sic = sem("s_sic")
        s_hT1 = sem("s_hT1")
        s_h = sem("s_h")
        s_relu = sem("s_relu")
        s_w = sem("s_w")
        s_scal = sem("s_scal")
        s_ft = sem("s_ft")
        s_prod = sem("s_prod")
        s_red = sem("s_red")
        s_msg = sem("s_msg")
        s_out = sem("s_out")

        def node_cols(t, q):
            return t[0:NP, q * CPP:(q + 1) * CPP, :]

        block = ctx.enter_context(nc.Block())

        @block.sync
        def _(sp):
            sp.dma_start(dst_i[:], dst_d).then_inc(s_in, 16)
            sp.dma_start(first_i[:], first_d.to_broadcast([P, GROUPS])).then_inc(s_in, 16)
            sp.dma_start(x_sb[0:NP, :, :], x_d.rearrange("(p c) f -> p c f", c=NC)).then_inc(s_xin, 16)
            sp.dma_start(w2[:], w2_d).then_inc(s_win, 16)
            sp.dma_start(w1[:], w1_d).then_inc(s_win, 16)
            sp.dma_start(b1[:], b1_d).then_inc(s_win, 16)
            sp.dma_start(si[:], si_d).then_inc(s_win, 16)

            for k in range(2):
                sp.dma_start(idx[k][:], src_d[k]).then_inc(s_idx[0][k], 16)
            sp.wait_ge(s_scaled, 1)
            sp.dma_start(y_d.rearrange("(p c) f -> p c f", c=NC), z_sb[0:NP, :, :]).then_inc(s_table[0], 16)

            def load_indices(layer, n, k, after):
                for j in range(GPC):
                    sp.wait_ge(s_g[layer][GPC * k + j], after)
                sp.dma_start(idx[k][:], src_d[n]).then_inc(s_idx[layer][k], 16)

            def load_edges(n, k):
                sp.dma_start(efT[k][:], efT_d[n]).then_inc(s_edge[k], 16)
                sp.dma_start(sh[k][:], sh_d[n]).then_inc(s_edge[k], 16)

            with sp.Fori(1, PAIRS) as i:
                for k in range(2):
                    load_indices(0, 2 * i + k, k, 16 * TPG * i)

            for k in range(2):
                load_edges(k, k)
                for j in range(GPC):
                    sp.wait_ge(s_g[0][GPC * k + j], 16 * TPG * PAIRS)
                sp.dma_start(idx[k][:], src_d[k]).then_inc(s_idx[1][k], 16)
            x1_v = x1_d.rearrange("(p c) f -> p c f", c=NC)
            for q in range(PIECES):
                sp.wait_ge(s_row[0], q + 1)
                sp.dma_start(x1_v[:, q * CPP:(q + 1) * CPP, :], node_cols(q_sb, q)).then_inc(s_table[1], 16)

            def reload_edges(i, k):
                sp.wait_ge(s_msg, 3 * (2 * i + k - 1))
                load_edges(2 * i + k, k)

            load_indices(1, 2, 0, 16 * TPG)
            with sp.Fori(1, PAIRS - 1) as i:
                load_indices(1, 2 * i + 1, 1, 16 * TPG * i)
                reload_edges(i, 0)
                load_indices(1, 2 * i + 2, 0, 16 * TPG * i + 16 * TPG)
                reload_edges(i, 1)
            load_indices(1, CHUNKS - 1, 1, 16 * TPG * (PAIRS - 1))
            for k in range(2):
                reload_edges(PAIRS - 1, k)

            full = n_out // NC
            rest = n_out - full * NC
            sent = 0
            for q in range(PIECES):
                sp.wait_ge(s_row[1], q + 1)
                a, b = q * CPP, (q + 1) * CPP
                sp.dma_start(out_d[0:full * NC, :].rearrange("(p c) f -> p c f", c=NC)[:, a:b, :],
                             q_sb[0:full, a:b, :]).then_inc(s_out, 16)
                sent += 1
                b = min(b, rest)
                if b > a:
                    sp.dma_start(out_d[full * NC + a:full * NC + b, :].rearrange("(p c) f -> p c f", p=1),
                                 q_sb[full:full + 1, a:b, :]).then_inc(s_out, 16)
                    sent += 1
            sp.wait_ge(s_out, 16 * sent)

        @block.gpsimd
        def _(pool):
            pool.iota(lane_i[:], [[1, WIDE]], base=0, channel_multiplier=0).then_inc(s_pool_c, 1)
            pool.memset(ident[:], 0.0).then_inc(s_pool_c, 1)
            pool.wait_ge(s_pool_c, 2)
            pool.affine_select(out=ident[:], in_=ident[:], compare_op=ALU.not_equal, fill=1.0, base=0,
                               pattern=[[-1, P]], channel_multiplier=1).then_inc(s_pool_c, 1)
            pool.memset(zero_b[:], 0.0).then_inc(s_pool_c, 1)
            pool.wait_ge(s_pool_c, 4)
            for b in range(2):
                pool.memset(hT[b][HID:P, :], 0.0).then_inc(s_hT1, 1)
                pool.wait_ge(s_hT1, 2 * b + 1)
                pool.memset(hT[b][HID:HID + 1, :], 1.0).then_inc(s_hT1, 1)
                pool.wait_ge(s_hT1, 2 * b + 2)
            pool.wait_ge(s_offsets, 2)
            pool.partition_all_reduce(spans[:], span[:], P, RMAX).then_inc(s_span, 1)

            def gather(layer, k, table, i, rows_used):
                pool.wait_ge(s_idx[layer][k], 16 * i + 16)
                for used, count in rows_used:
                    pool.wait_ge(used, count)
                pool.wait_ge(s_table[layer], 16 * (1 if layer == 0 else PIECES))
                pool.sem_inc(s_begun[layer], 1)
                for t in range(TPC):
                    pool.indirect_dma_start(
                        xg[k][:, t, :], None, table,
                        bass.IndirectOffsetOnAxis(ap=idx[k][:, t:t + 1], axis=0),
                    ).then_inc(s_g[layer][GPC * k + t // TPG], 16)

            for k in range(2):
                gather(0, k, y_d, 0, [])
            with pool.Fori(1, PAIRS) as i:
                for k in range(2):
                    gather(0, k, y_d, i, [(s_sum[0], 2 * i + k - 1)])
            for k in range(2):
                gather(1, k, x1_d, 0, [(s_sum[0], CHUNKS)])
            with pool.Fori(1, PAIRS) as i:
                for k in range(2):
                    gather(1, k, x1_d, i, [(s_ft, 4 * (2 * i + k - 1)), (s_scal, 2 * i + k - 1)])

        @block.scalar
        def _(act):
            act.wait_ge(s_maxdeg, 1)
            act.activation(root[0:NP, :], root[0:NP, :], ACT.Sqrt).then_inc(s_root, 1)

            def squares_and_deviations(layer):
                for q in range(PIECES):
                    act.wait_ge(s_cen[layer], q + 1)
                    act.activation(node_cols(q_sb, q), node_cols(z_sb, q), ACT.Square).then_inc(s_sq[layer], 1)
                act.wait_ge(s_var[layer], PIECES)
                act.activation(var[0:NP, :], var[0:NP, :], ACT.Sqrt, bias=eps[0:NP, :],
                               scale=1.0 / D).then_inc(s_std[layer], 1)

            squares_and_deviations(0)
            for q in range(PIECES):
                act.wait_ge(s_xt, q + 1)
                act.activation(x1T[:, q % 2, :, 0:NP],
                               ps_h[0].rearrange("p (b n) -> p b n", b=BPP)[:, :, 0:NP], ACT.Copy).then_inc(s_xtc, 1)
                act.wait_ge(s_si, q + 1)
                act.activation(node_cols(x_sb, q), ps_h[1][0:NP, :].rearrange("p (c f) -> p c f", f=D),
                               ACT.Copy).then_inc(s_sic, 1)

            def rectify(g, b, first):
                act.wait_ge(s_h, g + 1)
                if first:
                    act.wait_ge(s_win, 64)
                    act.wait_ge(s_hT1, 4)
                else:
                    act.wait_ge(s_w, g - 1)
                act.activation(hT[b][0:HID, :], ps_h[b][0:HID, :], ACT.Relu, bias=b1[:]).then_inc(s_relu, 1)

            def scalars(n, k, landed, first):
                for j in range(GPC):
                    act.wait_ge(s_g[1][GPC * k + j], landed)
                if not first:
                    act.wait_ge(s_red, GPC * (n - 1))
                act.activation(feat[k][:, :, MUL:2 * MUL], xg[k][:, :, 0:MUL], ACT.Copy).then_inc(s_scal, 1)

            for k in range(2):
                for j in range(GPC):
                    rectify(GPC * k + j, j % 2, k == 0 and j < 2)
                    if j == 0:
                        scalars(k, k, 16 * TPG, True)
            with act.Fori(1, PAIRS) as i:
                for k in range(2):
                    for j in range(GPC):
                        rectify(2 * GPC * i + GPC * k + j, j % 2, False)
                        if j == 0:
                            scalars(2 * i + k, k, 16 * TPG * i + 16 * TPG, False)
            squares_and_deviations(1)

        @block.tensor
        def _(pe):
            ohhi_v = ohhi[:, 0:NP * TPC].rearrange("p (c t) -> p c t", t=TPC)
            ohlo_v = ohlo[:, 0:NC * TPC].rearrange("p (c t) -> p c t", t=TPC)
            ohhi_w = ohhi[:, 2048:2048 + NP * TPC].rearrange("p (c t) -> p c t", t=TPC)
            ohlo_w = ohlo[:, 2048:2048 + NC * TPC].rearrange("p (c t) -> p c t", t=TPC)
            pe.wait_ge(s_pool_c, 4)
            pe.matmul(ps_deg, zero_b[:, 0:NP], zero_b[:, 0:NC], start=True, stop=False)
            with pe.Fori(0, PAIRS) as i:
                for k, (a, b) in enumerate(((ohhi_v, ohlo_v), (ohhi_w, ohlo_w))):
                    pe.wait_ge(s_doh, 4 * i + 2 * k + 2)
                    for t in range(TPC):
                        mm = pe.matmul(ps_deg, a[:, :, t], b[:, :, t], start=False, stop=False)
                    mm.then_inc(s_dmm, 1)
            pe.matmul(ps_deg, zero_b[:, 0:NP], zero_b[:, 0:NC], start=False, stop=True).then_inc(s_degree, 1)

            pe.wait_ge(s_near, 1)
            all_near = pe.value_load(near[0:1, 0:1], min_val=0, max_val=1)

            def window_sums(layer, rows, n, k, landed, first):
                if landed is None:
                    pe.wait_ge(s_msg, 3 * n + 3)
                else:
                    for j in range(GPC):
                        pe.wait_ge(s_g[0][GPC * k + j], landed)
                with pe.If(all_near == 1):
                    pe.wait_ge(s_oh[layer], n + 1)
                    if not first:
                        pe.wait_ge(s_acc[layer], GPC * (n - 1))
                    for j in range(GPC):
                        for t in range(TPG):
                            mm = pe.matmul(ps_sum[:, k, j, :], rows[:, TPG * j + t, :], oh[k][:, TPG * j + t, :],
                                           start=(t == 0), stop=(t == TPG - 1))
                    mm.then_inc(s_sum[layer], 1)
                with pe.Else():
                    HALVES = TPC // 2
                    with pe.Fori(0, WIDES) as v:
                        for m in range(HALVES):
                            pe.wait_ge(s_woh[layer], n * (WIDES * HALVES) + v * HALVES + m + 1)
                            for t in range(2):
                                mm = pe.matmul(ps_wide, rows[:, 2 * m + t, :], wide_oh[:, t, :],
                                               start=(m == 0 and t == 0), stop=(m == HALVES - 1 and t == 1))
                            mm.then_inc(s_wmm[layer], 1)
                    pe.wait_ge(s_wmm[layer], (n + 1) * (WIDES * HALVES) + 1)
                    pe.sem_inc(s_sum[layer], 1)

            def sums_to_rows(layer):
                pe.wait_ge(s_acc[layer], GPC * CHUNKS)
                for q in range(PIECES):
                    if q >= 4:
                        pe.wait_ge(s_ld[layer], q - 3)
                    for c in range(CPP):
                        col = q * CPP + c
                        mm = pe.transpose(ps[0:NP, q % 4, c * D:(c + 1) * D],
                                          sumT[:, col:NPAD:NC], ident[0:D, 0:D])
                    mm.then_inc(s_tr[layer], 1)

            for k in range(2):
                window_sums(0, xg[k], k, k, 16 * TPG, True)
            with pe.Fori(1, PAIRS) as i:
                for k in range(2):
                    window_sums(0, xg[k], 2 * i + k, k, 16 * TPG * i + 16 * TPG, False)
            sums_to_rows(0)

            pe.wait_ge(s_w2x, 4)
            for q in range(PIECES):
                pe.wait_ge(s_row[0], q + 1)
                if q >= 1:
                    pe.wait_ge(s_xtc, q)
                for b in range(BPP):
                    mm = pe.transpose(ps_h[0][:, b * P:b * P + NP],
                                      node_cols(q_sb, q).rearrange("p c f -> p (c f)")[:, b * P:(b + 1) * P],
                                      ident[0:NP, 0:NP])
                mm.then_inc(s_xt, 1)
                pe.wait_ge(s_xtc, q + 1)
                if q >= 1:
                    pe.wait_ge(s_sic, q)
                for b in range(BPP):
                    mm = pe.matmul(ps_h[1][0:NP, b * P:(b + 1) * P], x1T[:, q % 2, b, 0:NP], si[:],
                                   start=True, stop=True)
                mm.then_inc(s_si, 1)

            pe.wait_ge(s_sic, PIECES)

            def hidden(g, k, j, edges, first):
                if j == 0:
                    pe.wait_ge(s_edge[k], edges)
                if not first:
                    pe.wait_ge(s_relu, g - 1)
                pe.matmul(ps_h[j % 2][0:HID, :], w1[:, j, :], efT[k][:], start=True, stop=True).then_inc(s_h, 1)

            def weights(g, j, first):
                pe.wait_ge(s_relu, g + 1)
                if not first:
                    pe.wait_ge(s_prod, 4 * (g - 1))
                for t in range(TPG):
                    mm = pe.matmul(ps_w[j % 2][:, t, :], hT[j % 2][:, t * P:(t + 1) * P], w2[:],
                                   start=True, stop=True)
                mm.then_inc(s_w, 1)

            def chunk(n, k, edges, first):
                g = GPC * n
                for j in range(GPC):
                    hidden(g + j, k, j, edges, first and k == 0 and j < 2)
                    if not (first and k == 0 and j == 0):
                        weights(g + j - 1, (j - 1) % 2, first and k == 0 and j < 3)
                    if j == 2 and not (first and k == 0):
                        window_sums(1, msg[1 - k], n - 1, 1 - k, None, first)

            for k in range(2):
                chunk(k, k, 32, True)
            with pe.Fori(1, PAIRS) as i:
                for k in range(2):
                    chunk(2 * i + k, k, 32 * i + 32, False)
            weights(GPC * CHUNKS - 1, 1, False)
            window_sums(1, msg[1], CHUNKS - 1, 1, None, False)
            sums_to_rows(1)

        @block.vector
        def _(dve):
            steps = [0]

            def step(ins):
                steps[0] += 1
                ins.then_inc(s_dve_c, 1)
                dve.wait_ge(s_dve_c, steps[0])

            dve.wait_ge(s_in, 32)
            step(dve.tensor_scalar(part_i[:], dst_i[:], 7, None, ALU.logical_shift_right))
            step(dve.tensor_copy(hi[:], part_i[:]))
            step(dve.tensor_scalar(part_i[:], dst_i[:], P - 1, None, ALU.bitwise_and))
            step(dve.tensor_copy(lo[:], part_i[:]))
            dve.wait_ge(s_pool_c, 1)
            step(dve.tensor_copy(lane_f[:], lane_i[:]))
            step(dve.tensor_copy(lane[:], lane_f[:, 0:NC].unsqueeze(2).to_broadcast([P, NC, TPC])))

            def halves(t, k):
                return t[:, 2048 * k:2048 * (k + 1)].rearrange("p (c t) -> p c t", t=TPC)

            def degree_one_hots(i, k, n):
                cols = slice(n * TPC, n * TPC + TPC) if isinstance(n, int) else bass.ds(n * TPC, TPC)
                for v, m, oht in ((hi, NP, ohhi), (lo, NC, ohlo)):
                    dve.tensor_tensor(halves(oht, k)[:, 0:m, :], v[:, cols].unsqueeze(1).to_broadcast([P, m, TPC]),
                                      lane[:, 0:m, :], ALU.is_equal).then_inc(s_doh, 1)

            for k in range(2):
                degree_one_hots(0, k, k)
            with dve.Fori(1, PAIRS) as i:
                for k in range(2):
                    dve.wait_ge(s_dmm, 2 * i + k - 1)
                    degree_one_hots(i, k, 2 * i + k)

            step(dve.tensor_copy(dst_f[:], dst_i[:]))
            step(dve.tensor_copy(first_f[:], first_i[:]))
            step(dve.tensor_tensor(rel[:].rearrange("p (g t) -> p g t", t=TPG),
                                   dst_f[:].rearrange("p (g t) -> p g t", t=TPG),
                                   first_f[:].unsqueeze(2).to_broadcast([P, GROUPS, TPG]), ALU.subtract))
            step(dve.tensor_reduce(near_f[:, 0:1], rel[:], AX_X, ALU.min))
            dve.tensor_reduce(span[:, 0:1], rel[:], AX_X, ALU.max).then_inc(s_offsets, 1)
            dve.tensor_scalar(span[:, 1:2], near_f[:, 0:1], -1.0, None, ALU.mult).then_inc(s_offsets, 1)

            dve.wait_ge(s_degree, 1)
            step(dve.tensor_copy(deg[0:NP, :], ps_deg))
            dve.tensor_scalar(root[0:NP, :], deg[0:NP, :], 1.0, None, ALU.max).then_inc(s_maxdeg, 1)
            step(dve.tensor_scalar(mean[0:NP, :], deg[0:NP, :], 1.0, None, ALU.min))
            dve.wait_ge(s_root, 1)
            step(dve.reciprocal(deg[0:NP, :], root[0:NP, :]))
            step(dve.tensor_tensor(dinv[0:NP, :], deg[0:NP, :], mean[0:NP, :], ALU.mult))
            dve.wait_ge(s_xin, 16)
            dve.tensor_tensor(z_sb[0:NP, :, :], x_sb[0:NP, :, :], dinv[0:NP, :].unsqueeze(2).to_broadcast([NP, NC, D]),
                              ALU.mult).then_inc(s_scaled, 1)

            dve.wait_ge(s_span, 1)
            step(dve.tensor_scalar(near_f[:, 0:1], spans[:, 0:1], WIN - 0.5, None, ALU.is_le))
            step(dve.tensor_scalar(near_f[:, 1:2], spans[:, 1:2], 0.5, None, ALU.is_le))
            step(dve.tensor_tensor(near_f[:, 2:3], near_f[:, 0:1], near_f[:, 1:2], ALU.mult))
            dve.tensor_copy(near[:], near_f[:, 2:3]).then_inc(s_near, 1)
            dve.wait_ge(s_near, 1)
            all_near = dve.value_load(near[0:1, 0:1], min_val=0, max_val=1)

            dve.wait_ge(s_win, 64)
            dve.wait_ge(s_pool_c, 3)
            dve.memset(eps[:], EPS).then_inc(s_w2x, 1)
            dve.tensor_scalar(w2[:], w2[:], ALPHA, None, ALU.mult).then_inc(s_w2x, 1)
            dve.wait_ge(s_w2x, 2)
            dve.tensor_scalar(w2[:, 128:192], w2[:, 128:192], C110, None, ALU.mult).then_inc(s_w2x, 1)
            dve.scalar_tensor_tensor(out=si[:], in0=si[:], scalar=SI_SCALE, in1=ident[:], op0=ALU.mult,
                                     op1=ALU.add).then_inc(s_w2x, 1)

            def tiles(t, n, count, at=0):
                if isinstance(n, int):
                    return t[:, n * TPC + at:n * TPC + at + count]
                return t[:, bass.ds(n * TPC + at, count)]

            def one_hots(layer, n, k):
                dve.tensor_tensor(oh[k][:], tiles(rel, n, TPC).unsqueeze(2).to_broadcast([P, TPC, WIN]),
                                  lane_f[:, 0:WIN].unsqueeze(1).to_broadcast([P, TPC, WIN]),
                                  ALU.is_equal).then_inc(s_oh[layer], 1)

            def add_sums(layer, n, k):
                with dve.If(all_near == 1):
                    dve.wait_ge(s_sum[layer], n + 1)
                    for j in range(GPC):
                        col = GPC * n + j
                        at = first_i[0:1, col:col + 1] if isinstance(col, int) else first_i[0:1, bass.ds(col, 1)]
                        base = dve.value_load(at, min_val=0, max_val=n_out)
                        dve.wait_ge(s_acc[layer], GPC * n + j)
                        dve.tensor_tensor(sumT[:, bass.ds(base, WIN)], sumT[:, bass.ds(base, WIN)], ps_sum[:, k, j, :],
                                          ALU.add).then_inc(s_acc[layer], 1)

            def add_sums_general(layer, n, reduced=None):
                with dve.If(all_near == 0):
                    HALVES = TPC // 2
                    chain = (1 + 2 * WIDES) * n
                    if layer == 1:
                        dve.wait_ge(s_red, reduced)
                    dve.wait_ge(s_wadd[layer], chain)
                    dve.tensor_copy(wide_lane[:], lane_f[:]).then_inc(s_wadd[layer], 1)
                    with dve.Fori(0, WIDES) as v:
                        dve.wait_ge(s_wadd[layer], chain + 2 * v + 1)
                        for m in range(HALVES):
                            made = n * (WIDES * HALVES) + v * HALVES + m
                            dve.wait_ge(s_wmm[layer], made + 1)
                            dve.tensor_tensor(wide_oh, tiles(dst_f, n, 2, 2 * m).unsqueeze(2).to_broadcast([P, 2, WIDE]),
                                              wide_lane[:].unsqueeze(1).to_broadcast([P, 2, WIDE]),
                                              ALU.is_equal).then_inc(s_woh[layer], 1)
                        dve.wait_ge(s_woh[layer], made + 1)
                        dve.tensor_scalar(wide_lane[:], wide_lane[:], float(WIDE), None,
                                          ALU.add).then_inc(s_wadd[layer], 1)
                        dve.wait_ge(s_wmm[layer], made + 2)
                        at = bass.ds(v * WIDE, WIDE)
                        dve.tensor_tensor(sumT[:, at], sumT[:, at], ps_wide, ALU.add).then_inc(s_wadd[layer], 1)
                    dve.wait_ge(s_wadd[layer], chain + 2 * WIDES + 1)
                    dve.sem_inc(s_acc[layer], GPC)

            def normalise(layer):
                made = [0]

                def link(ins):
                    made[0] += 1
                    ins.then_inc(s_node[layer], 1)
                    return made[0]

                def cols(t, q):
                    return t[0:NP, q * CPP:(q + 1) * CPP]

                def spread(t, q):
                    return cols(t, q).unsqueeze(2).to_broadcast([NP, CPP, D])

                for q in range(PIECES):
                    dve.wait_ge(s_tr[layer], q + 1)
                    rows = ps[0:NP, q % 4, :].rearrange("p (c f) -> p c f", f=D)
                    other, op = (spread(dinv, q), ALU.mult) if layer == 0 else (node_cols(x_sb, q), ALU.add)
                    if layer == 1 and q == 0:
                        dve.wait_ge(s_sic, PIECES)
                    dve.tensor_tensor(node_cols(z_sb, q), rows, other, op).then_inc(s_ld[layer], 1)
                if layer == 0:
                    for q in range(PIECES):
                        dve.wait_ge(s_ld[layer], q + 1)
                        link(dve.tensor_tensor(node_cols(z_sb, q), node_cols(z_sb, q), node_cols(x_sb, q), ALU.add))
                for q in range(PIECES):
                    if layer == 0:
                        dve.wait_ge(s_node[layer], q + 1)
                    else:
                        dve.wait_ge(s_ld[layer], q + 1)
                    last = link(dve.tensor_reduce(cols(mean, q), node_cols(z_sb, q), AX_X, ALU.add))
                dve.wait_ge(s_node[layer], last)
                last = link(dve.tensor_scalar(mean[0:NP, :], mean[0:NP, :], 1.0 / D, None, ALU.mult))
                dve.wait_ge(s_node[layer], last)
                for q in range(PIECES):
                    dve.tensor_tensor(node_cols(z_sb, q), node_cols(z_sb, q), spread(mean, q),
                                      ALU.subtract).then_inc(s_cen[layer], 1)
                for q in range(PIECES):
                    dve.wait_ge(s_sq[layer], q + 1)
                    dve.tensor_reduce(cols(var, q), node_cols(q_sb, q), AX_X, ALU.add).then_inc(s_var[layer], 1)
                dve.wait_ge(s_std[layer], 1)
                last = link(dve.reciprocal(root[0:NP, :], var[0:NP, :]))
                dve.wait_ge(s_node[layer], last)
                for q in range(PIECES):
                    dve.tensor_tensor(node_cols(q_sb, q), node_cols(z_sb, q), spread(root, q),
                                      ALU.mult).then_inc(s_row[layer], 1)

            for layer in range(2):
                dve.sem_inc(s_wmm[layer], 1)
            dve.memset(sumT[:], 0.0).then_inc(s_zero, 1)
            one_hots(0, 0, 0)
            one_hots(0, 1, 1)
            dve.wait_ge(s_zero, 1)
            add_sums(0, 0, 0)
            add_sums_general(0, 0)
            with dve.Fori(1, PAIRS) as i:
                one_hots(0, 2 * i, 0)
                add_sums(0, 2 * i - 1, 1)
                add_sums_general(0, 2 * i - 1)
                one_hots(0, 2 * i + 1, 1)
                add_sums(0, 2 * i, 0)
                add_sums_general(0, 2 * i)
            add_sums(0, CHUNKS - 1, 1)
            add_sums_general(0, CHUNKS - 1)
            dve.wait_ge(s_scaled, 1)
            dve.wait_ge(s_table[0], 16)
            normalise(0)

            dve.wait_ge(s_tr[0], PIECES)
            dve.memset(sumT[:], 0.0).then_inc(s_zero, 1)
            dve.wait_ge(s_zero, 2)

            def features(n, k, landed, edges, first):
                for j in range(GPC):
                    dve.wait_ge(s_g[1][GPC * k + j], landed)
                dve.wait_ge(s_edge[k], edges)
                if not first:
                    dve.wait_ge(s_prod, 4 * GPC * n)
                sh0 = sh[k][:, :, 0:1]
                dve.tensor_tensor(feat[k][:, :, 0:MUL], xg[k][:, :, 0:MUL], sh0.to_broadcast([P, TPC, MUL]),
                                  ALU.mult).then_inc(s_ft, 1)
                dve.tensor_tensor(vec[:], xg[k][:, :, MUL:D], sh0.to_broadcast([P, TPC, 3 * MUL]),
                                  ALU.mult).then_inc(s_ft, 1)
                if not first:
                    dve.wait_ge(s_ft, 4 * n)
                dve.tensor_tensor(dots[:], xg[k][:, :, MUL:D].rearrange("p t (i m) -> p t i m", m=3),
                                  sh[k][:, :, 1:4].unsqueeze(2).to_broadcast([P, TPC, MUL, 3]),
                                  ALU.mult).then_inc(s_ft, 1)
                dve.wait_ge(s_ft, 4 * n + 3)
                dve.tensor_reduce(feat[k][:, :, 2 * MUL:3 * MUL], dots[:], AX_X, ALU.add).then_inc(s_ft, 1)

            def products(n, k, j, first):
                g = GPC * n + j
                b = j % 2
                dve.wait_ge(s_w, g + 1)
                if not first:
                    dve.wait_ge(s_red, g - 1)
                cut = slice(TPG * j, TPG * (j + 1))
                dve.tensor_tensor(
                    prod[b][:, :, 0:3].rearrange("p t c i o -> p t (c i) o"),
                    ps_w[b][:, :, 0:3 * MUL * MUL].rearrange("p t (c o) -> p t c o", o=MUL),
                    feat[k][:, cut, :].unsqueeze(3).to_broadcast([P, TPG, 3 * MUL, MUL]),
                    ALU.mult).then_inc(s_prod, 1)
                for m in range(3):
                    dve.tensor_tensor(
                        prod[b][:, :, 3 + m],
                        ps_w[b][:, :, 3 * MUL * MUL:].rearrange("p t (i o) -> p t i o", o=MUL),
                        vec[:, cut, m::3].unsqueeze(3).to_broadcast([P, TPG, MUL, MUL]),
                        ALU.mult).then_inc(s_prod, 1)

            def reduce_products(n, j):
                g = GPC * n + j
                dve.wait_ge(s_prod, 4 * g + 4)
                dve.tensor_reduce(
                    red[:, TPG * j:TPG * (j + 1)].rearrange("p t c o -> p (t c) o"),
                    prod[j % 2][:].rearrange("p t c i o -> p (t c) o i"),
                    AX_X, ALU.add).then_inc(s_red, 1)

            def messages(n, k):
                dve.wait_ge(s_red, GPC * n + GPC)
                dve.tensor_tensor(turned[:], red[:, :, 1].unsqueeze(3).to_broadcast([P, TPC, MUL, 3]),
                                  sh[k][:, :, 1:4].unsqueeze(2).to_broadcast([P, TPC, MUL, 3]),
                                  ALU.mult).then_inc(s_msg, 1)
                dve.tensor_tensor(msg[k][:, :, 0:MUL], red[:, :, 0], red[:, :, 2], ALU.add).then_inc(s_msg, 1)
                dve.wait_ge(s_msg, 3 * n + 1)
                dve.tensor_tensor(msg[k][:, :, MUL:D].rearrange("p t (o m) -> p t o m", m=3), turned[:],
                                  red[:, :, 3:6].rearrange("p t m o -> p t o m"), ALU.add).then_inc(s_msg, 1)

            def edge_chunk(n, k, landed, edges, first):
                one_hots(1, n, k)
                features(n, k, landed, edges, first and k == 0)
                dve.wait_ge(s_ft, 4 * n + 4)
                dve.wait_ge(s_scal, n + 1)
                if not (first and k == 0):
                    dve.wait_ge(s_msg, 3 * n)
                for j in range(GPC):
                    products(n, k, j, first and k == 0 and j < 2)
                    if j >= 1:
                        reduce_products(n, j - 1)
                    if j == 1 and not (first and k == 0):
                        add_sums_general(1, n - 1, GPC * n + 1)
                    if j == 2 and not (first and k == 0):
                        add_sums(1, n - 1, 1 - k)
                reduce_products(n, GPC - 1)
                messages(n, k)

            for k in range(2):
                edge_chunk(k, k, 16 * TPG, 32, True)
            with dve.Fori(1, PAIRS) as i:
                for k in range(2):
                    edge_chunk(2 * i + k, k, 16 * TPG * i + 16 * TPG, 32 * i + 32, False)
            add_sums(1, CHUNKS - 1, 1)
            add_sums_general(1, CHUNKS - 1, GPC * CHUNKS)
            normalise(1)


def kernel(**inputs):
    import numpy as np
    import concourse.bacc as bacc
    from concourse.bass_utils import run_bass_kernel_spmd

    x, src, dst = (np.asarray(inputs[n]) for n in ("x", "src", "dst"))
    ef, sh = np.asarray(inputs["edge_attr_32"]), np.asarray(inputs["edge_attr_4"])
    w1, b1 = np.asarray(inputs["L1_gnn_W1"]), np.asarray(inputs["L1_gnn_b1"])
    w2, b2 = np.asarray(inputs["L1_gnn_W2"]), np.asarray(inputs["L1_gnn_b2"])
    si0, si1 = np.asarray(inputs["L1_gnn_si_w0"]), np.asarray(inputs["L1_gnn_si_w1"])
    n, e = x.shape[0], src.shape[0]
    chunks = -(-e // (P * TPC))
    chunks += chunks % 2
    ep = chunks * P * TPC
    rows = -(-(n + 1) // P) * P

    def padded(a, count, value=0):
        out = np.full((count, *a.shape[1:]), value, a.dtype)
        out[:a.shape[0]] = a
        return out

    dst_p = padded(dst, ep, n)
    w1_g = np.zeros((P, GPC, HID), w1.dtype)
    for g in range(GPC):
        w1_g[D * g:D * (g + 1), g, :] = w1
    w2_p = np.zeros((P, WN), w2.dtype)
    for to, of in enumerate((0, 1, 3, 2)):
        w2_p[0:HID, 64 * to:64 * to + 64] = w2[:, 64 * of:64 * of + 64]
        w2_p[HID, 64 * to:64 * to + 64] = b2[64 * of:64 * of + 64]
    si_p = np.zeros((P, P), si0.dtype)
    for g in range(P // D):
        si_p[D * g:D * g + MUL, D * g:D * g + MUL] = si0
        for m in range(3):
            si_p[D * g + MUL + m:D * (g + 1):3, D * g + MUL + m:D * (g + 1):3] = si1
    arrays = {
        "x": padded(x, rows),
        "src": np.ascontiguousarray(padded(src, ep).reshape(chunks, TPC, P).transpose(0, 2, 1)),
        "dst": np.ascontiguousarray(dst_p.reshape(chunks * TPC, P).T),
        "first": np.ascontiguousarray(dst_p[::TPG * P].reshape(1, -1)),
        "efT": np.ascontiguousarray(padded(ef, ep).reshape(chunks, GPC, TPG * P, D).transpose(0, 1, 3, 2)
                                    .reshape(chunks, GPC * D, TPG * P)),
        "sh": np.ascontiguousarray(padded(sh, ep).reshape(chunks, TPC, P, 4).transpose(0, 2, 1, 3)),
        "w1": w1_g,
        "b1": np.ascontiguousarray(b1.reshape(-1, 1)),
        "w2": w2_p,
        "si": si_p,
    }
    nc = bacc.Bacc("TRN2", target_bir_lowering=False, num_devices=1)
    args = [nc.dram_tensor(f"in_{name}", a.shape, mybir.dt.from_np(a.dtype), kind="ExternalInput").ap()
            for name, a in arrays.items()]
    out = nc.dram_tensor("out_rows", (n, D), F32, kind="ExternalOutput").ap()
    gnn_program(nc, *args, out)
    r = run_bass_kernel_spmd(nc, [{f"in_{name}": a for name, a in arrays.items()}], core_ids=[0])
    return r.results[0]["out_rows"]
```
